# Optimizing a Trainium2 kernel written in Bass

```python
import numpy as np
import jax
import jax.numpy as jnp

def _softmax(x, axis=-1):
    return jax.nn.softmax(x, axis=axis)

def _gelu(x):
    return jax.nn.gelu(x, approximate=True)

def _silu(x):
    return jax.nn.silu(x)

def _sigmoid(x):
    return jax.nn.sigmoid(x)

def _layernorm(x, axis=-1, eps=1e-05):
    m = jnp.mean(x, axis=axis, keepdims=True)
    v = jnp.var(x, axis=axis, keepdims=True)
    return (x - m) / jnp.sqrt(v + eps)

def _scatter_add(tgt, idx, src, axis=0):
    return tgt.at[idx].add(src)

def _segment_sum(src, seg, n):
    return jax.ops.segment_sum(src, seg, n)
kernel_name = 'mk_dlrm_tower_d1_rec_r8_eec207'

def setup_inputs(seed: int=0):
    np.random.seed(seed)
    _w = jnp.asarray

    def _rec_inputs():
        import jax
        import jax.numpy as jnp
        _tk = jax.random.key(seed)
        dense_ctx = jax.random.normal(jax.random.fold_in(_tk, 190), (1024, 16), jnp.float32)
        ids = jnp.stack([jax.random.randint(jax.random.fold_in(_tk, 200 + f), (1024,), 0, v, jnp.int32) for f, v in enumerate([1250, 12500, 12500, 125000, 125000, 12500, 125000, 1250, 1000, 12500, 1000, 12500, 1250, 1000, 12500, 1250, 1000, 12500, 1000, 1250, 1250, 1000, 1000, 12500, 1000, 1250, 1250, 1250, 1000, 1000, 1000, 1000])], axis=1)
        tbl_0 = 0.05 * jax.random.normal(jax.random.fold_in(_tk, 500 + 0), (1250, 64), jnp.float32)
        tbl_1 = 0.05 * jax.random.normal(jax.random.fold_in(_tk, 500 + 1), (12500, 64), jnp.float32)
        tbl_2 = 0.05 * jax.random.normal(jax.random.fold_in(_tk, 500 + 2), (12500, 64), jnp.float32)
        tbl_3 = 0.05 * jax.random.normal(jax.random.fold_in(_tk, 500 + 3), (125000, 64), jnp.float32)
        tbl_4 = 0.05 * jax.random.normal(jax.random.fold_in(_tk, 500 + 4), (125000, 64), jnp.float32)
        tbl_5 = 0.05 * jax.random.normal(jax.random.fold_in(_tk, 500 + 5), (12500, 64), jnp.float32)
        tbl_6 = 0.05 * jax.random.normal(jax.random.fold_in(_tk, 500 + 6), (125000, 64), jnp.float32)
        tbl_7 = 0.05 * jax.random.normal(jax.random.fold_in(_tk, 500 + 7), (1250, 64), jnp.float32)
        tbl_8 = 0.05 * jax.random.normal(jax.random.fold_in(_tk, 500 + 8), (1000, 64), jnp.float32)
        tbl_9 = 0.05 * jax.random.normal(jax.random.fold_in(_tk, 500 + 9), (12500, 64), jnp.float32)
        tbl_10 = 0.05 * jax.random.normal(jax.random.fold_in(_tk, 500 + 10), (1000, 64), jnp.float32)
        tbl_11 = 0.05 * jax.random.normal(jax.random.fold_in(_tk, 500 + 11), (12500, 64), jnp.float32)
        tbl_12 = 0.05 * jax.random.normal(jax.random.fold_in(_tk, 500 + 12), (1250, 64), jnp.float32)
        tbl_13 = 0.05 * jax.random.normal(jax.random.fold_in(_tk, 500 + 13), (1000, 64), jnp.float32)
        tbl_14 = 0.05 * jax.random.normal(jax.random.fold_in(_tk, 500 + 14), (12500, 64), jnp.float32)
        tbl_15 = 0.05 * jax.random.normal(jax.random.fold_in(_tk, 500 + 15), (1250, 64), jnp.float32)
        tbl_16 = 0.05 * jax.random.normal(jax.random.fold_in(_tk, 500 + 16), (1000, 64), jnp.float32)
        tbl_17 = 0.05 * jax.random.normal(jax.random.fold_in(_tk, 500 + 17), (12500, 64), jnp.float32)
        tbl_18 = 0.05 * jax.random.normal(jax.random.fold_in(_tk, 500 + 18), (1000, 64), jnp.float32)
        tbl_19 = 0.05 * jax.random.normal(jax.random.fold_in(_tk, 500 + 19), (1250, 64), jnp.float32)
        tbl_20 = 0.05 * jax.random.normal(jax.random.fold_in(_tk, 500 + 20), (1250, 64), jnp.float32)
        tbl_21 = 0.05 * jax.random.normal(jax.random.fold_in(_tk, 500 + 21), (1000, 64), jnp.float32)
        tbl_22 = 0.05 * jax.random.normal(jax.random.fold_in(_tk, 500 + 22), (1000, 64), jnp.float32)
        tbl_23 = 0.05 * jax.random.normal(jax.random.fold_in(_tk, 500 + 23), (12500, 64), jnp.float32)
        tbl_24 = 0.05 * jax.random.normal(jax.random.fold_in(_tk, 500 + 24), (1000, 64), jnp.float32)
        tbl_25 = 0.05 * jax.random.normal(jax.random.fold_in(_tk, 500 + 25), (1250, 64), jnp.float32)
        tbl_26 = 0.05 * jax.random.normal(jax.random.fold_in(_tk, 500 + 26), (1250, 64), jnp.float32)
        tbl_27 = 0.05 * jax.random.normal(jax.random.fold_in(_tk, 500 + 27), (1250, 64), jnp.float32)
        tbl_28 = 0.05 * jax.random.normal(jax.random.fold_in(_tk, 500 + 28), (1000, 64), jnp.float32)
        tbl_29 = 0.05 * jax.random.normal(jax.random.fold_in(_tk, 500 + 29), (1000, 64), jnp.float32)
        tbl_30 = 0.05 * jax.random.normal(jax.random.fold_in(_tk, 500 + 30), (1000, 64), jnp.float32)
        tbl_31 = 0.05 * jax.random.normal(jax.random.fold_in(_tk, 500 + 31), (1000, 64), jnp.float32)
        _rk = jax.random.fold_in(_tk, 7)
        W_top1 = 0.0693375 * jax.random.normal(jax.random.fold_in(_tk, 801), (208, 512), jnp.float32)
        W_top2 = 0.0441942 * jax.random.normal(jax.random.fold_in(_tk, 802), (512, 256), jnp.float32)
        W_top3 = 0.0625 * jax.random.normal(jax.random.fold_in(_tk, 803), (256, 1), jnp.float32)
        b_top1 = jnp.zeros((512,), jnp.float32)
        b_top2 = jnp.zeros((256,), jnp.float32)
        return (dense_ctx, ids, tbl_0, tbl_1, tbl_2, tbl_3, tbl_4, tbl_5, tbl_6, tbl_7, tbl_8, tbl_9, tbl_10, tbl_11, tbl_12, tbl_13, tbl_14, tbl_15, tbl_16, tbl_17, tbl_18, tbl_19, tbl_20, tbl_21, tbl_22, tbl_23, tbl_24, tbl_25, tbl_26, tbl_27, tbl_28, tbl_29, tbl_30, tbl_31, W_top1, b_top1, W_top2, b_top2, W_top3)
    dense_ctx, ids, tbl_0, tbl_1, tbl_2, tbl_3, tbl_4, tbl_5, tbl_6, tbl_7, tbl_8, tbl_9, tbl_10, tbl_11, tbl_12, tbl_13, tbl_14, tbl_15, tbl_16, tbl_17, tbl_18, tbl_19, tbl_20, tbl_21, tbl_22, tbl_23, tbl_24, tbl_25, tbl_26, tbl_27, tbl_28, tbl_29, tbl_30, tbl_31, W_top1, b_top1, W_top2, b_top2, W_top3 = _rec_inputs()

    def _L0_rec_setup():
        import jax, jax.numpy as jnp
        import numpy as np
        F0 = 32
        D = 64
        B = 256

        def _cin_layer(h, h0, W, b):
            Hn = h.shape[1]
            Mn = h0.shape[1]
            Wr = W.reshape(W.shape[0], Hn, Mn)
            x = jnp.einsum('bhd,bmd,ohm->bod', h, h0, Wr) + b[None, :, None]
            return jax.nn.relu(x)
        key = jax.random.key(seed)
        k1, k2, k3 = jax.random.split(key, 3)
        inputs = jax.random.normal(k1, (B, F0, D), dtype=jnp.float32)
        W1 = jax.random.normal(k2, (128, F0 * F0), dtype=jnp.float32) * (1.0 / np.sqrt(F0 * F0))
        b1 = jnp.zeros((128,), dtype=jnp.float32)
        W2 = jax.random.normal(k3, (128, 64 * F0), dtype=jnp.float32) * (1.0 / np.sqrt(64 * F0))
        b2 = jnp.zeros((128,), dtype=jnp.float32)
        return {'inputs': inputs, 'W1': W1, 'b1': b1, 'W2': W2, 'b2': b2}
    _L0_rec_all = _L0_rec_setup()
    _L0_rec_in = {k: v for k, v in _L0_rec_all.items() if k in ('W1', 'b1', 'W2', 'b2')}
    del _L0_rec_all
    return {'dense_ctx': dense_ctx, 'ids': ids, 'tbl_0': tbl_0, 'tbl_1': tbl_1, 'tbl_2': tbl_2, 'tbl_3': tbl_3, 'tbl_4': tbl_4, 'tbl_5': tbl_5, 'tbl_6': tbl_6, 'tbl_7': tbl_7, 'tbl_8': tbl_8, 'tbl_9': tbl_9, 'tbl_10': tbl_10, 'tbl_11': tbl_11, 'tbl_12': tbl_12, 'tbl_13': tbl_13, 'tbl_14': tbl_14, 'tbl_15': tbl_15, 'tbl_16': tbl_16, 'tbl_17': tbl_17, 'tbl_18': tbl_18, 'tbl_19': tbl_19, 'tbl_20': tbl_20, 'tbl_21': tbl_21, 'tbl_22': tbl_22, 'tbl_23': tbl_23, 'tbl_24': tbl_24, 'tbl_25': tbl_25, 'tbl_26': tbl_26, 'tbl_27': tbl_27, 'tbl_28': tbl_28, 'tbl_29': tbl_29, 'tbl_30': tbl_30, 'tbl_31': tbl_31, 'W_top1': W_top1, 'b_top1': b_top1, 'W_top2': W_top2, 'b_top2': b_top2, 'W_top3': W_top3, 'L0_rec_W1': _L0_rec_in['W1'], 'L0_rec_b1': _L0_rec_in['b1'], 'L0_rec_W2': _L0_rec_in['W2'], 'L0_rec_b2': _L0_rec_in['b2']}

def reference(dense_ctx, ids, tbl_0, tbl_1, tbl_2, tbl_3, tbl_4, tbl_5, tbl_6, tbl_7, tbl_8, tbl_9, tbl_10, tbl_11, tbl_12, tbl_13, tbl_14, tbl_15, tbl_16, tbl_17, tbl_18, tbl_19, tbl_20, tbl_21, tbl_22, tbl_23, tbl_24, tbl_25, tbl_26, tbl_27, tbl_28, tbl_29, tbl_30, tbl_31, W_top1, b_top1, W_top2, b_top2, W_top3, L0_rec_W1, L0_rec_b1, L0_rec_W2, L0_rec_b2):
    import jax
    import jax.numpy as jnp

    def _L0_rec_ref(inputs, W1, b1, W2, b2):
        import jax, jax.numpy as jnp
        import numpy as np
        F0 = 32
        D = 64
        B = 256

        def _cin_layer(h, h0, W, b):
            Hn = h.shape[1]
            Mn = h0.shape[1]
            Wr = W.reshape(W.shape[0], Hn, Mn)
            x = jnp.einsum('bhd,bmd,ohm->bod', h, h0, Wr) + b[None, :, None]
            return jax.nn.relu(x)
        h0 = inputs
        x1 = _cin_layer(h0, h0, W1, b1)
        next_hidden = x1[:, :64]
        direct1 = x1[:, 64:]
        direct2 = _cin_layer(next_hidden, h0, W2, b2)
        result = jnp.concatenate([direct1, direct2], axis=1)
        return jnp.sum(result, axis=-1)
    e = jnp.stack([tbl_0[ids[:, 0]], tbl_1[ids[:, 1]], tbl_2[ids[:, 2]], tbl_3[ids[:, 3]], tbl_4[ids[:, 4]], tbl_5[ids[:, 5]], tbl_6[ids[:, 6]], tbl_7[ids[:, 7]], tbl_8[ids[:, 8]], tbl_9[ids[:, 9]], tbl_10[ids[:, 10]], tbl_11[ids[:, 11]], tbl_12[ids[:, 12]], tbl_13[ids[:, 13]], tbl_14[ids[:, 14]], tbl_15[ids[:, 15]], tbl_16[ids[:, 16]], tbl_17[ids[:, 17]], tbl_18[ids[:, 18]], tbl_19[ids[:, 19]], tbl_20[ids[:, 20]], tbl_21[ids[:, 21]], tbl_22[ids[:, 22]], tbl_23[ids[:, 23]], tbl_24[ids[:, 24]], tbl_25[ids[:, 25]], tbl_26[ids[:, 26]], tbl_27[ids[:, 27]], tbl_28[ids[:, 28]], tbl_29[ids[:, 29]], tbl_30[ids[:, 30]], tbl_31[ids[:, 31]]], axis=1)
    z = _L0_rec_ref(e, L0_rec_W1, L0_rec_b1, L0_rec_W2, L0_rec_b2)
    z = z.reshape(z.shape[0], -1)
    h = jnp.concatenate([z, dense_ctx], axis=1)
    h = jnp.maximum(h @ W_top1 + b_top1, 0.0)
    h = jnp.maximum(h @ W_top2 + b_top2, 0.0)
    y = h @ W_top3
    return y

_drawn_inputs = setup_inputs


def setup_inputs(seed=0):
    import zlib

    import numpy as np

    out = dict(_drawn_inputs(seed))
    spreads = {'b_top1': (0.0, 2.0),
     'b_top2': (0.0, 2.0),
     'L0_rec_b1': (0.0, 0.326),
     'L0_rec_b2': (0.0, 0.719)}
    factors = {'tbl_0': 8.0,
     'tbl_1': 8.0,
     'tbl_2': 8.0,
     'tbl_3': 8.0,
     'tbl_4': 8.0,
     'tbl_5': 8.0,
     'tbl_6': 8.0,
     'tbl_7': 8.0,
     'tbl_8': 8.0,
     'tbl_9': 8.0,
     'tbl_10': 8.0,
     'tbl_11': 8.0,
     'tbl_12': 8.0,
     'tbl_13': 8.0,
     'tbl_14': 8.0,
     'tbl_15': 8.0,
     'tbl_16': 8.0,
     'tbl_17': 8.0,
     'tbl_18': 8.0,
     'tbl_19': 8.0,
     'tbl_20': 8.0,
     'tbl_21': 8.0,
     'tbl_22': 8.0,
     'tbl_23': 8.0,
     'tbl_24': 8.0,
     'tbl_25': 8.0,
     'tbl_26': 8.0,
     'tbl_27': 8.0,
     'tbl_28': 8.0,
     'tbl_29': 8.0,
     'tbl_30': 8.0,
     'tbl_31': 8.0,
     'L0_rec_W1': 8.0,
     'L0_rec_W2': 8.0,
     'dense_ctx': 8.0}
    for name, (base, spread) in spreads.items():
        noise = np.random.default_rng([zlib.crc32(name.encode()), seed]).standard_normal(out[name].shape)
        drawn = base * np.exp(spread * noise) if base else spread * noise
        out[name] = jnp.asarray(drawn.astype(out[name].dtype))
    for name, factor in factors.items():
        out[name] = (out[name] * factor).astype(out[name].dtype)
    return out
```

```python
import concourse.bass as bass
from concourse import mybir
from contextlib import ExitStack

B = 1024
F = 32
D = 64
O = 128
H = 64
DENSE = 16
HID1, HID2 = 512, 256

P = 128
CB = 8
N = CB * D
CHUNKS = B // CB
BT = B // P
PAIRS = CHUNKS // 2
PAIRS_PER_BT = P // CB // 2
WRAP = F + F // 2
ROW = B * D
SH = P // F
K1 = (F // 2) // SH
HALF = F // 2
GH, GM = 16, 8
NI, NJ = H // GH, F // GM


def build_dlrm(nc, a):
    fp32 = mybir.dt.float32
    i32 = mybir.dt.int32
    ALU = mybir.AluOpType
    ACT = mybir.ActivationFunctionType

    ctx = ExitStack()
    with ctx:
        def sb(name, shape, dt=fp32):
            return ctx.enter_context(nc.sbuf_tensor(name, shape, dt))

        def ps(name, shape):
            return ctx.enter_context(nc.psum_tensor(name, shape, fp32))

        def sem(name):
            return ctx.enter_context(nc.semaphore(name))

        emb = nc.dram_tensor("emb_rows", [WRAP, ROW], fp32, kind="Internal")

        idx = sb("idx", [P, F], i32)
        gathered = sb("gathered", [P, F, D])
        w1n = sb("w1n", [P, F * F])
        w2n = sb("w2n", [P, H * F])
        w1fold = sb("w1fold", [P, (K1 * SH) * F + HALF])
        w1T = sb("w1T", [P, K1 + 1, O])
        w2T = sb("w2T", [P, NI * NJ, O])
        bias1 = sb("bias1", [P, 1])
        bias2 = sb("bias2", [P, 1])
        ident = sb("ident", [P, P])
        h0 = [sb(f"h0_{s}", [P, N]) for s in range(2)]
        h0shift = [sb(f"h0shift_{s}", [P, K1, N]) for s in range(2)]
        h0half = [sb(f"h0half_{s}", [HALF, N]) for s in range(2)]
        prod1 = [sb(f"prod1_{s}", [P, K1, N]) for s in range(2)]
        prod1h = [sb(f"prod1h_{s}", [HALF, N]) for s in range(2)]
        x1 = [sb(f"x1_{s}", [P, N]) for s in range(2)]
        x1rep = [sb(f"x1rep_{s}", [P, NI, N]) for s in range(2)]
        h0rep = [sb(f"h0rep_{s}", [P, NJ, N]) for s in range(2)]
        prod2 = [sb(f"prod2_{s}", [P, NJ, N]) for s in range(2)]
        z1 = sb("z1", [P, B])
        z2 = sb("z2", [P, B])
        dense_n = sb("dense_n", [P, BT, DENSE])
        denseT = sb("denseT", [DENSE, B])
        wt1a = sb("wt1a", [P, HID1])
        wt1b = sb("wt1b", [P, HID1])
        wt1c = sb("wt1c", [DENSE, HID1])
        wt2 = sb("wt2", [P, HID1 // P, HID2])
        wt3 = sb("wt3", [P, HID2 // P])
        bt1 = sb("bt1", [P, HID1 // P])
        bt2 = sb("bt2", [P, HID2 // P])
        hid1 = sb("hid1", [P, HID1 // P, N])
        hid2 = sb("hid2", [P, HID2 // P, N])
        y = sb("y", [1, B])

        acc1 = [ps(f"acc1_{s}", [P, N]) for s in range(2)]
        acc2 = [ps(f"acc2_{s}", [P, N]) for s in range(2)]
        tp = [ps(f"tp_{s}", [P, N]) for s in range(2)]

        weights_in = sem("weights_in")
        idx_in = sem("idx_in")
        tiles_begun = sem("tiles_begun")
        rows_gathered = sem("rows_gathered")
        emb_stored = sem("emb_stored")
        ident_zero = sem("ident_zero")
        ident_ready = sem("ident_ready")
        weights_grouped = sem("weights_grouped")
        tp_filled = sem("tp_filled")
        tp_copied = sem("tp_copied")
        h0_in = [sem(f"h0_in_{s}") for s in range(2)]
        h0rep_in = [sem(f"h0rep_in_{s}") for s in range(2)]
        x1rep_in = [sem(f"x1rep_in_{s}") for s in range(2)]
        prod1_ready = sem("prod1_ready")
        prod2_ready = sem("prod2_ready")
        acc1_ready = sem("acc1_ready")
        prod2_used = sem("prod2_used")
        x1_ready = sem("x1_ready")
        z2_ready = sem("z2_ready")
        hid1_mm = sem("hid1_mm")
        hid1_ready = sem("hid1_ready")
        hid2_mm = sem("hid2_mm")
        hid2_ready = sem("hid2_ready")
        y_mm = sem("y_mm")
        y_ready = sem("y_ready")
        y_stored = sem("y_stored")

        WEIGHT_DMAS = 12

        w2r = prod2[0][:, :, :].rearrange("o i (j hm) -> o i j hm", j=NJ)

        transposes = [(w1fold[:, k * P:(k + 1) * P], w1T[:, k, :], P) for k in range(K1)]
        transposes += [(w1fold[:, K1 * P:K1 * P + HALF], w1T[0:HALF, K1, :], HALF)]
        transposes += [(w2r[:, i, j, :], w2T[:, NJ * i + j, :], P) for i in range(NI) for j in range(NJ)]
        transposes += [(dense_n[:, t, :], denseT[:, t * P:(t + 1) * P], DENSE) for t in range(BT)]

        def software_pipeline(eng, step):
            step(0, 0, 0, True, False)
            step(1, 0, 1, True, False)
            with eng.Fori(1, PAIRS - 1) as pair:
                step(2 * pair, pair, 0, False, False)
                step(2 * pair + 1, pair, 1, False, False)
            step(CHUNKS - 2, PAIRS - 1, 0, False, True)
            step(CHUNKS - 1, PAIRS - 1, 1, False, True)

        block = ctx.enter_context(nc.Block())

        @block.gpsimd
        def _(pool):
            nc.gpsimd.memset(ident[:, :], 0.0).then_inc(ident_zero, 1)
            pool.wait_ge(ident_zero, 1)
            nc.gpsimd.affine_select(out=ident[:, :], in_=ident[:, :], compare_op=ALU.not_equal, fill=1.0,
                                    base=0, pattern=[[-1, P]], channel_multiplier=1).then_inc(ident_ready, 1)
            with pool.Fori(0, BT) as t:
                pool.dma_start(idx[:, :], a["ids"][bass.ds(t * P, P), :]).then_inc(idx_in, 16)
                pool.wait_ge(idx_in, 16 * t + 16)
                pool.sem_inc(tiles_begun, 1)
                for f in range(F):
                    nc.gpsimd.indirect_dma_start(
                        out=gathered[:, f, :], out_offset=None, in_=a[f"tbl_{f}"],
                        in_offset=bass.IndirectOffsetOnAxis(ap=idx[:, f:f + 1], axis=0)).then_inc(rows_gathered, 16)
                pool.wait_ge(rows_gathered, 16 * F * t + 16 * F)
                for f0, f1, r0 in ((0, F, 0), (0, WRAP - F, F)):
                    dst = bass.AP(emb, r0 * ROW + t * (P * D), [[D, P], [ROW, f1 - f0], [1, D]])
                    pool.dma_start(dst, gathered[:, f0:f1, :]).then_inc(emb_stored, 16)
                pool.wait_ge(emb_stored, 32 * t + 32)

        @block.sync
        def _(sp):
            sp.dma_start(w1n[:, :], a["L0_rec_W1"]).then_inc(weights_in, 16)
            sp.dma_start(w2n[:, :], a["L0_rec_W2"]).then_inc(weights_in, 16)
            sp.dma_start(bias1[:, :], a["L0_rec_b1"].rearrange("(p one) -> p one", one=1)).then_inc(weights_in, 16)
            sp.dma_start(bias2[:, :], a["L0_rec_b2"].rearrange("(p one) -> p one", one=1)).then_inc(weights_in, 16)
            sp.dma_start(dense_n[:, :, :], a["dense_ctx"].rearrange("(t p) c -> p t c", p=P)).then_inc(weights_in, 16)
            sp.dma_start(wt1a[H:P, :], a["W_top1"][0:O - H, :]).then_inc(weights_in, 16)
            sp.dma_start(wt1b[:, :], a["W_top1"][O - H:2 * O - H, :]).then_inc(weights_in, 16)
            sp.dma_start(wt1c[:, :], a["W_top1"][2 * O - H:2 * O - H + DENSE, :]).then_inc(weights_in, 16)
            sp.dma_start(wt2[:, :, :], a["W_top2"].rearrange("(k p) n -> p k n", p=P)).then_inc(weights_in, 16)
            with nc.allow_non_contiguous_dma(reason="short columns of biases"):
                sp.dma_start(wt3[:, :], a["W_top3"].rearrange("(k p) one -> p (k one)", p=P)).then_inc(weights_in, 16)
                sp.dma_start(bt1[:, :], a["b_top1"].rearrange("(k p) -> p k", p=P)).then_inc(weights_in, 16)
                sp.dma_start(bt2[:, :], a["b_top2"].rearrange("(k p) -> p k", p=P)).then_inc(weights_in, 16)

            def load_h0(col, s):
                sp.dma_start(h0[s][:, :], bass.AP(emb, col, [[0, SH], [ROW, F], [1, N]])).then_inc(h0_in[s], 16)
                for k in range(K1):
                    src = bass.AP(emb, SH * k * ROW + col, [[ROW, SH], [ROW, F], [1, N]])
                    sp.dma_start(h0shift[s][:, k, :], src).then_inc(h0_in[s], 16)
                sp.dma_start(h0half[s][:, :], bass.AP(emb, HALF * ROW + col, [[ROW, HALF], [1, N]])).then_inc(h0_in[s], 16)

            def load_h0rep(col, s):
                for j in range(NJ):
                    src = bass.AP(emb, GM * j * ROW + col, [[0, GH], [ROW, GM], [1, N]])
                    sp.dma_start(h0rep[s][:, j, :], src).then_inc(h0rep_in[s], 16)

            def replicate_x1(s):
                for i in range(NI):
                    src = x1[s][GH * i:GH * (i + 1), :].unsqueeze(1).to_broadcast([GH, GM, N])
                    sp.dma_start(x1rep[s][:, i, :], src).then_inc(x1rep_in[s], 16)

            sp.wait_ge(emb_stored, 32)
            load_h0(0, 0)
            load_h0(N, 1)
            load_h0rep(0, 0)
            load_h0rep(N, 1)
            sp.wait_ge(x1_ready, 1)
            replicate_x1(0)

            def step(c, pair, s, first, last):
                if not last and s == 0:
                    sp.wait_ge(emb_stored, ((pair + 1) // PAIRS_PER_BT) * 32 + 32)
                if first and s == 0:
                    sp.wait_ge(prod1_ready, 1)
                else:
                    sp.wait_ge(prod2_ready, NI * c)
                if not last:
                    load_h0((c + 2) * N, s)
                if not (last and s == 1):
                    sp.wait_ge(x1_ready, c + 2)
                    replicate_x1(1 - s)
                if not last:
                    sp.wait_ge(prod2_ready, NI * c + NI)
                    load_h0rep((c + 2) * N, s)

            software_pipeline(sp, step)

            sp.wait_ge(y_ready, 2)
            sp.dma_start(a["out"].rearrange("b one -> one b"), y[:, :]).then_inc(y_stored, 16)
            sp.wait_ge(y_stored, 16)

        @block.vector
        def _(dve):
            dve.wait_ge(weights_in, 16 * WEIGHT_DMAS)
            for s in range(K1 * SH + 1):
                n0 = HALF if s == HALF else F - s
                for i0, n in ((0, n0), (n0, F - n0)):
                    if n == 0 or (s == HALF and i0):
                        continue
                    m0 = (i0 + s) % F
                    ij, ji = i0 * F + m0, m0 * F + i0
                    dst = w1fold[:, s * F + i0:s * F + i0 + n]
                    x = w1n[:, ij:ij + (n - 1) * (F + 1) + 1:F + 1]
                    if s == 0:
                        last = nc.vector.tensor_copy(dst, x)
                    else:
                        last = nc.vector.tensor_tensor(dst, x, w1n[:, ji:ji + (n - 1) * (F + 1) + 1:F + 1], ALU.add)
            for i in range(NI):
                for j in range(NJ):
                    src = w2n[:, :].rearrange("o (i hh jm) -> o i hh jm", i=NI, hh=GH)[:, i, :, GM * j:GM * (j + 1)]
                    last = nc.vector.tensor_copy(w2r[:, i, j, :].rearrange("o (hh mm) -> o hh mm", hh=GH), src)
            last.then_inc(weights_grouped, 1)
            for n, (_, dst, rows) in enumerate(transposes):
                dve.wait_ge(tp_filled, n + 1)
                nc.vector.tensor_copy(dst, tp[n % 2][0:rows, 0:P]).then_inc(tp_copied, 1)

            def products1(c, pair, s):
                dve.wait_ge(h0_in[s], 16 * (K1 + 2) * pair + 16 * (K1 + 2))
                nc.vector.tensor_tensor(prod1[s][:, :, :], h0shift[s][:, :, :],
                                        h0[s][:, :].unsqueeze(1).to_broadcast([P, K1, N]), ALU.mult)
                nc.vector.tensor_tensor(prod1h[s][:, :], h0half[s][:, :], h0[s][0:HALF, :],
                                        ALU.mult).then_inc(prod1_ready, 1)

            products1(0, 0, 0)

            def step(c, pair, s, first, last):
                if not (last and s == 1):
                    dve.wait_ge(acc1_ready, c)
                    products1(c + 1, pair + s, 1 - s)
                dve.wait_ge(h0rep_in[s], 16 * NJ * pair + 16 * NJ)
                dve.wait_ge(x1rep_in[s], 16 * NI * pair + 16 * NI)
                for i in range(NI):
                    if not (first and s == 0 and i < 2):
                        dve.wait_ge(prod2_used, NI * c + (i - 1))
                    nc.vector.tensor_tensor(prod2[i % 2][:, :, :], h0rep[s][:, :, :],
                                            x1rep[s][:, i, :].unsqueeze(1).to_broadcast([P, NJ, N]),
                                            ALU.mult).then_inc(prod2_ready, 1)

            software_pipeline(dve, step)

        @block.tensor
        def _(pe):
            pe.wait_ge(weights_in, 16 * WEIGHT_DMAS)
            pe.wait_ge(ident_ready, 1)
            pe.wait_ge(weights_grouped, 1)
            for n, (src, _, rows) in enumerate(transposes):
                if n >= 2:
                    pe.wait_ge(tp_copied, n - 1)
                nc.tensor.transpose(tp[n % 2][0:rows, 0:P], src, ident[:, :]).then_inc(tp_filled, 1)
            pe.wait_ge(tp_copied, len(transposes))

            def layer1(s):
                for k in range(K1):
                    nc.tensor.matmul(acc1[s][:, :], w1T[:, k, :], prod1[s][:, k, :], start=(k == 0), stop=False)
                nc.tensor.matmul(acc1[s][:, :], w1T[0:HALF, K1, :], prod1h[s][:, :],
                                 start=False, stop=True).then_inc(acc1_ready, 1)

            pe.wait_ge(prod1_ready, 1)
            layer1(0)

            def step(c, pair, s, first, last):
                if not (last and s == 1):
                    pe.wait_ge(prod1_ready, c + 2)
                    pe.wait_ge(x1_ready, c)
                    layer1(1 - s)
                if not first:
                    pe.wait_ge(z2_ready, c - 1)
                for i in range(NI):
                    pe.wait_ge(prod2_ready, NI * c + (i + 1))
                    for j in range(NJ):
                        mm = nc.tensor.matmul(acc2[s][:, :], w2T[:, NJ * i + j, :], prod2[i % 2][:, j, :],
                                              start=(i == 0 and j == 0), stop=(i == NI - 1 and j == NJ - 1))
                    mm.then_inc(prod2_used, 1)

            software_pipeline(pe, step)

            pe.wait_ge(x1_ready, CHUNKS)
            pe.wait_ge(z2_ready, CHUNKS)
            for half in range(2):
                cols = slice(half * N, (half + 1) * N)
                for m in range(HID1 // P):
                    n = half * (HID1 // P) + m
                    mc = slice(m * P, (m + 1) * P)
                    if n >= 2:
                        pe.wait_ge(hid1_ready, n - 1)
                    nc.tensor.matmul(acc1[m % 2][:, :], wt1b[:, mc], z2[:, cols], start=True, stop=False)
                    nc.tensor.matmul(acc1[m % 2][:, :], wt1a[H:P, mc], z1[H:P, cols], start=False, stop=False)
                    nc.tensor.matmul(acc1[m % 2][:, :], wt1c[:, mc], denseT[:, cols], start=False,
                                     stop=True).then_inc(hid1_mm, 1)
                pe.wait_ge(hid1_ready, (half + 1) * (HID1 // P))
                for m in range(HID2 // P):
                    if half:
                        pe.wait_ge(hid2_ready, half * (HID2 // P))
                    for k in range(HID1 // P):
                        mm = nc.tensor.matmul(acc2[m % 2][:, :], wt2[:, k, m * P:(m + 1) * P], hid1[:, k, :],
                                              start=(k == 0), stop=(k == HID1 // P - 1))
                    mm.then_inc(hid2_mm, 1)
                pe.wait_ge(hid2_ready, (half + 1) * (HID2 // P))
                for k in range(HID2 // P):
                    mm = nc.tensor.matmul(tp[half][0:1, :], wt3[:, k:k + 1], hid2[:, k, :],
                                          start=(k == 0), stop=(k == HID2 // P - 1))
                mm.then_inc(y_mm, 1)

        @block.scalar
        def _(act):
            def reduce_relu(acc, bias, out, z, c, ready):
                for b in range(CB):
                    cols = slice(b * D, (b + 1) * D)
                    ins = nc.scalar.activation(out[:, cols], acc[:, cols], ACT.Relu, bias=bias[:, :],
                                               accum_out=z[:, bass.ds(c * CB + b, 1)])
                ins.then_inc(ready, 1)

            act.wait_ge(weights_in, 16 * WEIGHT_DMAS)
            act.wait_ge(acc1_ready, 1)
            reduce_relu(acc1[0], bias1, x1[0], z1, 0, x1_ready)

            def step(c, pair, s, first, last):
                if not (last and s == 1):
                    act.wait_ge(acc1_ready, c + 2)
                    if not (first and s == 0):
                        act.wait_ge(x1rep_in[1 - s], 16 * NI * (pair + s))
                    reduce_relu(acc1[1 - s], bias1, x1[1 - s], z1, c + 1, x1_ready)
                act.wait_ge(prod2_used, NI * c + NI)
                reduce_relu(acc2[s], bias2, acc2[s], z2, c, z2_ready)

            software_pipeline(act, step)

            for half in range(2):
                for m in range(HID1 // P):
                    n = half * (HID1 // P) + m
                    act.wait_ge(hid1_mm, n + 1)
                    if half and m == 0:
                        act.wait_ge(hid2_mm, HID2 // P)
                    nc.scalar.activation(hid1[:, m, :], acc1[m % 2][:, :], ACT.Relu,
                                         bias=bt1[:, m:m + 1]).then_inc(hid1_ready, 1)
                for m in range(HID2 // P):
                    act.wait_ge(hid2_mm, half * (HID2 // P) + m + 1)
                    if half and m == 0:
                        act.wait_ge(y_mm, 1)
                    nc.scalar.activation(hid2[:, m, :], acc2[m % 2][:, :], ACT.Relu,
                                         bias=bt2[:, m:m + 1]).then_inc(hid2_ready, 1)
                act.wait_ge(y_mm, half + 1)
                nc.scalar.copy(y[0:1, half * N:(half + 1) * N], tp[half][0:1, :]).then_inc(y_ready, 1)


def kernel(**inputs):
    import numpy as _np
    import concourse.bacc as _bacc
    from concourse import mybir as _mybir
    from concourse.bass_utils import run_bass_kernel_spmd as _run

    nc = _bacc.Bacc("TRN2", target_bir_lowering=False, num_devices=1)
    arrays, aps = {}, {}
    for name, value in inputs.items():
        v = _np.ascontiguousarray(value)
        arrays[f"in_{name}"] = v
        aps[name] = nc.dram_tensor(f"in_{name}", v.shape, _mybir.dt.from_np(v.dtype), kind="ExternalInput").ap()
    aps["out"] = nc.dram_tensor("out_y", (B, 1), _mybir.dt.float32, kind="ExternalOutput").ap()
    build_dlrm(nc, aps)
    r = _run(nc, [arrays], core_ids=[0])
    return r.results[0]["out_y"]
```

```python
import concourse.bass as bass
from concourse import mybir
from contextlib import ExitStack

B = 1024
F = 32
D = 64
O = 128
H = 64
DENSE = 16
HID1, HID2 = 512, 256

P = 128
CB = 8
N = CB * D
CHUNKS = B // CB
BT = B // P
PAIRS = CHUNKS // 2
PAIRS_PER_BT = P // CB // 2
WRAP = F + F // 2
ROW = B * D
SH = P // F
K1 = (F // 2) // SH
HALF = F // 2
GH, GM = 16, 8
NI, NJ = H // GH, F // GM
PLAIN, SPLIT = (0, 2), (1, 3)
REM = 2 * HALF


def build_dlrm(nc, a):
    fp32 = mybir.dt.float32
    fp32r = mybir.dt.float32r
    i32 = mybir.dt.int32
    ALU = mybir.AluOpType
    ACT = mybir.ActivationFunctionType

    ctx = ExitStack()
    with ctx:
        def sb(name, shape, dt=fp32):
            return ctx.enter_context(nc.sbuf_tensor(name, shape, dt))

        def ps(name, shape):
            return ctx.enter_context(nc.psum_tensor(name, shape, fp32))

        def sem(name):
            return ctx.enter_context(nc.semaphore(name))

        emb = nc.dram_tensor("emb_rows", [WRAP, ROW], fp32, kind="Internal")

        idx = sb("idx", [P, F], i32)
        gathered = sb("gathered", [P, F, D])
        w1T = sb("w1T", [P, K1, O])
        w1remT = [sb(f"w1remT_{s}", [3 * REM, O], fp32r) for s in range(2)]
        w2T = sb("w2T", [P, len(PLAIN) * NJ, O])
        w2hi = sb("w2hi", [P, len(SPLIT) * NJ, O], fp32r)
        w2lo = sb("w2lo", [P, len(SPLIT) * NJ, O], fp32r)
        w16hi = sb("w16hi", [P, HALF], fp32r)
        bias1 = sb("bias1", [P, 1])
        bias2 = sb("bias2", [P, 1])
        ident = sb("ident", [P, P])
        h0 = [sb(f"h0_{s}", [P, N]) for s in range(2)]
        h0shift = [sb(f"h0shift_{s}", [P, K1, N]) for s in range(2)]
        rem_a = sb("rem_a", [REM, N])
        rem_b = sb("rem_b", [REM, N])
        rem_prod = sb("rem_prod", [REM, N])
        rem_parts = sb("rem_parts", [3 * REM, N], fp32r)
        prod1 = [sb(f"prod1_{s}", [P, K1, N]) for s in range(2)]
        x1 = [sb(f"x1_{s}", [P, N]) for s in range(2)]
        x1rep = [sb(f"x1rep_{s}", [P, NI, N]) for s in range(2)]
        h0rep = [sb(f"h0rep_{s}", [P, NJ, N]) for s in range(2)]
        prod2 = [sb(f"prod2_{n}", [P, NJ, N]) for n in range(len(PLAIN))]
        prod2s = [sb(f"prod2s_{n}", [P, NJ, N]) for n in range(len(SPLIT))]
        prod2hi = [sb(f"prod2hi_{n}", [P, NJ, N], fp32r) for n in range(len(SPLIT))]
        prod2lo = [sb(f"prod2lo_{n}", [P, NJ, N], fp32r) for n in range(len(SPLIT))]
        z1 = sb("z1", [P, B])
        z2 = sb("z2", [P, B])
        dense_n = sb("dense_n", [P, BT, DENSE])
        denseT = sb("denseT", [DENSE, B])
        wt1a = sb("wt1a", [P, HID1])
        wt1b = sb("wt1b", [P, HID1])
        wt1c = sb("wt1c", [DENSE, HID1])
        wt2 = sb("wt2", [P, HID1 // P, HID2])
        wt3 = sb("wt3", [P, HID2 // P])
        bt1 = sb("bt1", [P, HID1 // P])
        bt2 = sb("bt2", [P, HID2 // P])
        hid1 = sb("hid1", [P, HID1 // P, N])
        hid2 = sb("hid2", [P, HID2 // P, N])
        y = sb("y", [1, B])

        acc1 = [ps(f"acc1_{s}", [P, N]) for s in range(2)]
        acc2 = [ps(f"acc2_{s}", [P, N]) for s in range(2)]
        tp = [ps(f"tp_{s}", [P, N]) for s in range(2)]

        weights_in = sem("weights_in")
        idx_in = sem("idx_in")
        tiles_begun = sem("tiles_begun")
        rows_gathered = sem("rows_gathered")
        emb_stored = sem("emb_stored")
        ident_zero = sem("ident_zero")
        ident_ready = sem("ident_ready")
        weights_grouped = sem("weights_grouped")
        weight_step = sem("weight_step")
        tp_filled = sem("tp_filled")
        tp_copied = sem("tp_copied")
        h0_in = [sem(f"h0_in_{s}") for s in range(2)]
        h0rep_in = [sem(f"h0rep_in_{s}") for s in range(2)]
        x1rep_in = [sem(f"x1rep_in_{s}") for s in range(2)]
        rem_in = sem("rem_in")
        rem_prod_ready = sem("rem_prod_ready")
        rem_hi_ready = sem("rem_hi_ready")
        prod1_ready = sem("prod1_ready")
        plain_ready = sem("plain_ready")
        split_ready = sem("split_ready")
        hi_ready = sem("hi_ready")
        lo_ready = sem("lo_ready")
        plain_used = sem("plain_used")
        split_used = sem("split_used")
        acc1_ready = sem("acc1_ready")
        x1_ready = sem("x1_ready")
        z2_ready = sem("z2_ready")
        hid1_mm = sem("hid1_mm")
        hid1_ready = sem("hid1_ready")
        hid2_mm = sem("hid2_mm")
        hid2_ready = sem("hid2_ready")
        y_mm = sem("y_mm")
        y_ready = sem("y_ready")
        y_stored = sem("y_stored")

        WEIGHT_DMAS = 12

        w1n = x1rep[0][:, 0:2, :].rearrange("o a n -> o (a n)")
        w2n = x1rep[1][:, :, :].rearrange("o a n -> o (a n)")
        w1fold = x1rep[0][:, 2, :]
        w16 = x1rep[0][:, 3, 0:HALF]
        w1rem = [x1rep[0][:, 3, P * (s + 1):P * (s + 1) + 3 * REM] for s in range(2)]
        w2r = prod2[0][:, :, :].rearrange("o i (j hm) -> o i j hm", j=NJ)

        transposes = [(w1fold[:, k * P:(k + 1) * P], P, w1T[:, k, :], None) for k in range(K1)]
        transposes += [(w1rem[s], 3 * REM, w1remT[s][:, :], None) for s in range(2)]
        for n, i in enumerate(PLAIN):
            transposes += [(w2r[:, i, j, :], P, w2T[:, NJ * n + j, :], None) for j in range(NJ)]
        for n, i in enumerate(SPLIT):
            transposes += [(w2r[:, i, j, :], P, w2hi[:, NJ * n + j, :], w2lo[:, NJ * n + j, :]) for j in range(NJ)]
        transposes += [(dense_n[:, t, :], DENSE, denseT[:, t * P:(t + 1) * P], None) for t in range(BT)]

        def software_pipeline(eng, step):
            step(0, 0, 0, True, False)
            step(1, 0, 1, True, False)
            with eng.Fori(1, PAIRS - 1) as pair:
                step(2 * pair, pair, 0, False, False)
                step(2 * pair + 1, pair, 1, False, False)
            step(CHUNKS - 2, PAIRS - 1, 0, False, True)
            step(CHUNKS - 1, PAIRS - 1, 1, False, True)

        block = ctx.enter_context(nc.Block())

        @block.gpsimd
        def _(pool):
            nc.gpsimd.memset(ident[:, :], 0.0).then_inc(ident_zero, 1)
            pool.wait_ge(ident_zero, 1)
            nc.gpsimd.affine_select(out=ident[:, :], in_=ident[:, :], compare_op=ALU.not_equal, fill=1.0,
                                    base=0, pattern=[[-1, P]], channel_multiplier=1).then_inc(ident_ready, 1)
            with pool.Fori(0, BT) as t:
                pool.dma_start(idx[:, :], a["ids"][bass.ds(t * P, P), :]).then_inc(idx_in, 16)
                pool.wait_ge(idx_in, 16 * t + 16)
                pool.sem_inc(tiles_begun, 1)
                for f in range(F):
                    nc.gpsimd.indirect_dma_start(
                        out=gathered[:, f, :], out_offset=None, in_=a[f"tbl_{f}"],
                        in_offset=bass.IndirectOffsetOnAxis(ap=idx[:, f:f + 1], axis=0)).then_inc(rows_gathered, 16)
                pool.wait_ge(rows_gathered, 16 * F * t + 16 * F)
                for f0, f1, r0 in ((0, F, 0), (0, WRAP - F, F)):
                    dst = bass.AP(emb, r0 * ROW + t * (P * D), [[D, P], [ROW, f1 - f0], [1, D]])
                    pool.dma_start(dst, gathered[:, f0:f1, :]).then_inc(emb_stored, 16)
                pool.wait_ge(emb_stored, 32 * t + 32)

        @block.sync
        def _(sp):
            sp.dma_start(w1n, a["L0_rec_W1"]).then_inc(weights_in, 16)
            sp.dma_start(w2n, a["L0_rec_W2"]).then_inc(weights_in, 16)
            sp.dma_start(bias1[:, :], a["L0_rec_b1"].rearrange("(p one) -> p one", one=1)).then_inc(weights_in, 16)
            sp.dma_start(bias2[:, :], a["L0_rec_b2"].rearrange("(p one) -> p one", one=1)).then_inc(weights_in, 16)
            sp.dma_start(dense_n[:, :, :], a["dense_ctx"].rearrange("(t p) c -> p t c", p=P)).then_inc(weights_in, 16)
            sp.dma_start(wt1a[H:P, :], a["W_top1"][0:O - H, :]).then_inc(weights_in, 16)
            sp.dma_start(wt1b[:, :], a["W_top1"][O - H:2 * O - H, :]).then_inc(weights_in, 16)
            sp.dma_start(wt1c[:, :], a["W_top1"][2 * O - H:2 * O - H + DENSE, :]).then_inc(weights_in, 16)
            sp.dma_start(wt2[:, :, :], a["W_top2"].rearrange("(k p) n -> p k n", p=P)).then_inc(weights_in, 16)
            with nc.allow_non_contiguous_dma(reason="short columns of biases"):
                sp.dma_start(wt3[:, :], a["W_top3"].rearrange("(k p) one -> p (k one)", p=P)).then_inc(weights_in, 16)
                sp.dma_start(bt1[:, :], a["b_top1"].rearrange("(k p) -> p k", p=P)).then_inc(weights_in, 16)
                sp.dma_start(bt2[:, :], a["b_top2"].rearrange("(k p) -> p k", p=P)).then_inc(weights_in, 16)

            def load_h0(col, s):
                sp.dma_start(h0[s][:, :], bass.AP(emb, col, [[0, SH], [ROW, F], [1, N]])).then_inc(h0_in[s], 16)
                for k in range(K1):
                    src = bass.AP(emb, SH * k * ROW + col, [[ROW, SH], [ROW, F], [1, N]])
                    sp.dma_start(h0shift[s][:, k, :], src).then_inc(h0_in[s], 16)

            def load_rem(col):
                for t, f0 in ((rem_a, 0), (rem_b, HALF)):
                    src = bass.AP(emb, f0 * ROW + col, [[N, 2], [ROW, HALF], [1, N]])
                    sp.dma_start(t[:, :], src).then_inc(rem_in, 16)

            def load_h0rep(col, s):
                for j in range(NJ):
                    src = bass.AP(emb, GM * j * ROW + col, [[0, GH], [ROW, GM], [1, N]])
                    sp.dma_start(h0rep[s][:, j, :], src).then_inc(h0rep_in[s], 16)

            def replicate_x1(s):
                for i in range(NI):
                    src = x1[s][GH * i:GH * (i + 1), :].unsqueeze(1).to_broadcast([GH, GM, N])
                    sp.dma_start(x1rep[s][:, i, :], src).then_inc(x1rep_in[s], 16)

            sp.wait_ge(emb_stored, 32)
            load_rem(0)
            load_h0(0, 0)
            load_h0(N, 1)
            load_h0rep(0, 0)
            load_h0rep(N, 1)
            sp.wait_ge(x1_ready, 1)
            replicate_x1(0)

            def step(c, pair, s, first, last):
                if not last and s == 0:
                    sp.wait_ge(emb_stored, ((pair + 1) // PAIRS_PER_BT) * 32 + 32)
                if first and s == 0:
                    sp.wait_ge(prod1_ready, 1)
                else:
                    sp.wait_ge(plain_ready, len(PLAIN) * c)
                if not last:
                    load_h0((c + 2) * N, s)
                    if s == 0:
                        load_rem((c + 2) * N)
                if not (last and s == 1):
                    sp.wait_ge(x1_ready, c + 2)
                    replicate_x1(1 - s)
                if not last:
                    sp.wait_ge(plain_ready, len(PLAIN) * c + len(PLAIN))
                    load_h0rep((c + 2) * N, s)

            software_pipeline(sp, step)

            sp.wait_ge(y_ready, 2)
            sp.dma_start(a["out"].rearrange("b one -> one b"), y[:, :]).then_inc(y_stored, 16)
            sp.wait_ge(y_stored, 16)

        @block.vector
        def _(dve):
            dve.wait_ge(weights_in, 16 * WEIGHT_DMAS)
            for s in range(K1 * SH):
                for i0, n in ((0, F - s), (F - s, s)):
                    if n == 0:
                        continue
                    m0 = (i0 + s) % F
                    ij, ji = i0 * F + m0, m0 * F + i0
                    dst = w1fold[:, s * F + i0:s * F + i0 + n]
                    x = w1n[:, ij:ij + (n - 1) * (F + 1) + 1:F + 1]
                    if s == 0:
                        nc.vector.tensor_copy(dst, x)
                    else:
                        nc.vector.tensor_tensor(dst, x, w1n[:, ji:ji + (n - 1) * (F + 1) + 1:F + 1], ALU.add)
            ij, ji = HALF, HALF * F
            nc.vector.tensor_tensor(w16, w1n[:, ij:ij + (HALF - 1) * (F + 1) + 1:F + 1],
                                    w1n[:, ji:ji + (HALF - 1) * (F + 1) + 1:F + 1], ALU.add).then_inc(weight_step, 1)
            for s in range(2):
                last = nc.vector.memset(w1rem[s], 0.0)
            last.then_inc(weight_step, 1)
            dve.wait_ge(weight_step, 2)
            nc.vector.tensor_copy(w16hi[:, :], w16).then_inc(weight_step, 1)
            dve.wait_ge(weight_step, 3)
            for u in range(2):
                c0 = HALF * u
                nc.vector.tensor_copy(w1rem[u][:, c0:c0 + HALF], w16hi[:, :].bitcast(fp32))
                nc.vector.tensor_tensor(w1rem[u][:, REM + c0:REM + c0 + HALF], w16, w16hi[:, :].bitcast(fp32),
                                        ALU.subtract)
                nc.vector.tensor_copy(w1rem[u][:, 2 * REM + c0:2 * REM + c0 + HALF], w16hi[:, :].bitcast(fp32))
            for i in range(NI):
                for j in range(NJ):
                    src = w2n.rearrange("o (i hh jm) -> o i hh jm", i=NI, hh=GH)[:, i, :, GM * j:GM * (j + 1)]
                    last = nc.vector.tensor_copy(w2r[:, i, j, :].rearrange("o (hh mm) -> o hh mm", hh=GH), src)
            last.then_inc(weights_grouped, 1)
            parts = 0
            for n, (_, rows, dst, lo) in enumerate(transposes):
                dve.wait_ge(tp_filled, n + 1)
                src = tp[n % 2][0:rows, 0:P]
                if lo is None:
                    nc.vector.tensor_copy(dst, src).then_inc(tp_copied, 1)
                else:
                    parts += 1
                    nc.vector.tensor_copy(dst, src).then_inc(weight_step, 1)
                    dve.wait_ge(weight_step, 3 + parts)
                    nc.vector.tensor_tensor(lo, src, dst.bitcast(fp32), ALU.subtract).then_inc(tp_copied, 1)

            def remainder_products(pair):
                dve.wait_ge(rem_in, 32 * pair + 32)
                nc.vector.tensor_tensor(rem_prod[:, :], rem_a[:, :], rem_b[:, :], ALU.mult).then_inc(rem_prod_ready, 1)

            def products1(pair, s):
                dve.wait_ge(h0_in[s], 16 * (K1 + 1) * pair + 16 * (K1 + 1))
                return nc.vector.tensor_tensor(prod1[s][:, :, :], h0shift[s][:, :, :],
                                               h0[s][:, :].unsqueeze(1).to_broadcast([P, K1, N]), ALU.mult)

            def remainder_lo(pair):
                dve.wait_ge(rem_hi_ready, pair + 1)
                return nc.vector.tensor_tensor(rem_parts[2 * REM:3 * REM, :], rem_prod[:, :],
                                               rem_parts[0:REM, :].bitcast(fp32), ALU.subtract)

            remainder_products(0)
            products1(0, 0)
            remainder_lo(0).then_inc(prod1_ready, 1)

            def step(c, pair, s, first, last):
                if not last and s == 1:
                    dve.wait_ge(acc1_ready, c + 1)
                    remainder_products(pair + 1)
                    products1(pair + 1, 0)
                    remainder_lo(pair + 1).then_inc(prod1_ready, 1)
                elif s == 0:
                    if not first:
                        dve.wait_ge(acc1_ready, c)
                    products1(pair, 1).then_inc(prod1_ready, 1)
                dve.wait_ge(h0rep_in[s], 16 * NJ * pair + 16 * NJ)
                dve.wait_ge(x1rep_in[s], 16 * NI * pair + 16 * NI)

                def products2(dst, i):
                    return nc.vector.tensor_tensor(dst[:, :, :], h0rep[s][:, :, :],
                                                   x1rep[s][:, i, :].unsqueeze(1).to_broadcast([P, NJ, N]), ALU.mult)

                for n in range(2):
                    if not (first and s == 0):
                        dve.wait_ge(lo_ready, 2 * c + (n - 1))
                    products2(prod2s[n], SPLIT[n]).then_inc(split_ready, 1)
                    if not (first and s == 0):
                        dve.wait_ge(plain_used, 2 * c + (n - 1))
                    products2(prod2[n], PLAIN[n]).then_inc(plain_ready, 1)
                    dve.wait_ge(hi_ready, 2 * c + (n + 1))
                    nc.vector.tensor_tensor(prod2lo[n][:, :, :], prod2s[n][:, :, :], prod2hi[n][:, :, :].bitcast(fp32),
                                            ALU.subtract).then_inc(lo_ready, 1)

            software_pipeline(dve, step)

        @block.tensor
        def _(pe):
            pe.wait_ge(weights_in, 16 * WEIGHT_DMAS)
            pe.wait_ge(ident_ready, 1)
            pe.wait_ge(weights_grouped, 1)
            for n, (src, rows, _, _) in enumerate(transposes):
                if n >= 2:
                    pe.wait_ge(tp_copied, n - 1)
                nc.tensor.transpose(tp[n % 2][0:rows, 0:P], src, ident[:, :]).then_inc(tp_filled, 1)
            pe.wait_ge(tp_copied, len(transposes))

            def layer1(s):
                for k in range(K1):
                    nc.tensor.matmul(acc1[s][:, :], w1T[:, k, :], prod1[s][:, k, :], start=(k == 0), stop=False)
                nc.tensor.matmul(acc1[s][:, :], w1remT[s][:, :], rem_parts[:, :],
                                 start=False, stop=True).then_inc(acc1_ready, 1)

            pe.wait_ge(prod1_ready, 1)
            layer1(0)

            def step(c, pair, s, first, last):
                if not (last and s == 1):
                    pe.wait_ge(prod1_ready, c + 2)
                    if not (first and s == 0):
                        pe.wait_ge(x1_ready, c)
                    layer1(1 - s)
                if not first:
                    pe.wait_ge(z2_ready, c - 1)
                for n in range(2):
                    pe.wait_ge(plain_ready, 2 * c + (n + 1))
                    for j in range(NJ):
                        mm = nc.tensor.matmul(acc2[s][:, :], w2T[:, NJ * n + j, :], prod2[n][:, j, :],
                                              start=(n == 0 and j == 0), stop=False)
                    mm.then_inc(plain_used, 1)
                    pe.wait_ge(lo_ready, 2 * c + (n + 1))
                    for j in range(NJ):
                        k = NJ * n + j
                        nc.tensor.matmul(acc2[s][:, :], w2lo[:, k, :], prod2hi[n][:, j, :], start=False, stop=False)
                        nc.tensor.matmul(acc2[s][:, :], w2hi[:, k, :], prod2lo[n][:, j, :], start=False, stop=False)
                        mm = nc.tensor.matmul(acc2[s][:, :], w2hi[:, k, :], prod2hi[n][:, j, :],
                                              start=False, stop=(n == 1 and j == NJ - 1))
                    mm.then_inc(split_used, 1)

            software_pipeline(pe, step)

            pe.wait_ge(x1_ready, CHUNKS)
            pe.wait_ge(z2_ready, CHUNKS)
            for half in range(2):
                cols = slice(half * N, (half + 1) * N)
                for m in range(HID1 // P):
                    n = half * (HID1 // P) + m
                    mc = slice(m * P, (m + 1) * P)
                    if n >= 2:
                        pe.wait_ge(hid1_ready, n - 1)
                    nc.tensor.matmul(acc1[m % 2][:, :], wt1b[:, mc], z2[:, cols], start=True, stop=False)
                    nc.tensor.matmul(acc1[m % 2][:, :], wt1a[H:P, mc], z1[H:P, cols], start=False, stop=False)
                    nc.tensor.matmul(acc1[m % 2][:, :], wt1c[:, mc], denseT[:, cols], start=False,
                                     stop=True).then_inc(hid1_mm, 1)
                pe.wait_ge(hid1_ready, (half + 1) * (HID1 // P))
                for m in range(HID2 // P):
                    if half:
                        pe.wait_ge(hid2_ready, half * (HID2 // P))
                    for k in range(HID1 // P):
                        mm = nc.tensor.matmul(acc2[m % 2][:, :], wt2[:, k, m * P:(m + 1) * P], hid1[:, k, :],
                                              start=(k == 0), stop=(k == HID1 // P - 1))
                    mm.then_inc(hid2_mm, 1)
                pe.wait_ge(hid2_ready, (half + 1) * (HID2 // P))
                for k in range(HID2 // P):
                    mm = nc.tensor.matmul(tp[half][0:1, :], wt3[:, k:k + 1], hid2[:, k, :],
                                          start=(k == 0), stop=(k == HID2 // P - 1))
                mm.then_inc(y_mm, 1)

        @block.scalar
        def _(act):
            def reduce_relu(acc, bias, out, z, c, ready):
                for b in range(CB):
                    cols = slice(b * D, (b + 1) * D)
                    ins = nc.scalar.activation(out[:, cols], acc[:, cols], ACT.Relu, bias=bias[:, :],
                                               accum_out=z[:, bass.ds(c * CB + b, 1)])
                ins.then_inc(ready, 1)

            def remainder_hi(pair):
                act.wait_ge(rem_prod_ready, pair + 1)
                nc.scalar.copy(rem_parts[0:REM, :], rem_prod[:, :])
                nc.scalar.copy(rem_parts[REM:2 * REM, :], rem_prod[:, :]).then_inc(rem_hi_ready, 1)

            act.wait_ge(weights_in, 16 * WEIGHT_DMAS)
            remainder_hi(0)
            act.wait_ge(acc1_ready, 1)
            reduce_relu(acc1[0], bias1, x1[0], z1, 0, x1_ready)

            def step(c, pair, s, first, last):
                def product_hi(n):
                    act.wait_ge(split_ready, 2 * c + (n + 1))
                    if not (first and s == 0):
                        act.wait_ge(split_used, 2 * c + (n - 1))
                    nc.scalar.copy(prod2hi[n][:, :, :], prod2s[n][:, :, :]).then_inc(hi_ready, 1)

                if not last and s == 1:
                    remainder_hi(pair + 1)
                product_hi(0)
                if not (first and s == 0):
                    act.wait_ge(split_used, 2 * c)
                    reduce_relu(acc2[1 - s], bias2, acc2[1 - s], z2, c - 1, z2_ready)
                if not (last and s == 1):
                    act.wait_ge(acc1_ready, c + 2)
                    if not (first and s == 0):
                        act.wait_ge(x1rep_in[1 - s], 16 * NI * (pair + s))
                    reduce_relu(acc1[1 - s], bias1, x1[1 - s], z1, c + 1, x1_ready)
                product_hi(1)

            software_pipeline(act, step)
            act.wait_ge(split_used, 2 * CHUNKS)
            reduce_relu(acc2[1], bias2, acc2[1], z2, CHUNKS - 1, z2_ready)

            for half in range(2):
                for m in range(HID1 // P):
                    n = half * (HID1 // P) + m
                    act.wait_ge(hid1_mm, n + 1)
                    if half and m == 0:
                        act.wait_ge(hid2_mm, HID2 // P)
                    nc.scalar.activation(hid1[:, m, :], acc1[m % 2][:, :], ACT.Relu,
                                         bias=bt1[:, m:m + 1]).then_inc(hid1_ready, 1)
                for m in range(HID2 // P):
                    act.wait_ge(hid2_mm, half * (HID2 // P) + m + 1)
                    if half and m == 0:
                        act.wait_ge(y_mm, 1)
                    nc.scalar.activation(hid2[:, m, :], acc2[m % 2][:, :], ACT.Relu,
                                         bias=bt2[:, m:m + 1]).then_inc(hid2_ready, 1)
                act.wait_ge(y_mm, half + 1)
                nc.scalar.copy(y[0:1, half * N:(half + 1) * N], tp[half][0:1, :]).then_inc(y_ready, 1)


def kernel(**inputs):
    import numpy as _np
    import concourse.bacc as _bacc
    from concourse import mybir as _mybir
    from concourse.bass_utils import run_bass_kernel_spmd as _run

    nc = _bacc.Bacc("TRN2", target_bir_lowering=False, num_devices=1)
    arrays, aps = {}, {}
    for name, value in inputs.items():
        v = _np.ascontiguousarray(value)
        arrays[f"in_{name}"] = v
        aps[name] = nc.dram_tensor(f"in_{name}", v.shape, _mybir.dt.from_np(v.dtype), kind="ExternalInput").ap()
    aps["out"] = nc.dram_tensor("out_y", (B, 1), _mybir.dt.float32, kind="ExternalOutput").ap()
    build_dlrm(nc, aps)
    r = _run(nc, [arrays], core_ids=[0])
    return r.results[0]["out_y"]
```

```python
import concourse.bass as bass
from concourse import mybir
from contextlib import ExitStack

B = 1024
F = 32
D = 64
O = 128
H = 64
DENSE = 16
HID1, HID2 = 512, 256
M1, M2 = HID1 // 128, HID2 // 128

P = 128
CB = 8
N = CB * D
CHUNKS = B // CB
PAIRS = CHUNKS // 2
BT = B // P
GS = P // F
PAIR_GATHERS = 2 * CB // GS
WRAP = F + F // 2
ROW = B * D + 1024
SH = P // F
K1 = (F // 2) // SH
HALF = F // 2
GH, GM = 16, 8
NI, NJ = H // GH, F // GM
PLAIN, SPLIT = (0, 2), (1, 3)
SPLIT_J = ((NJ, NJ - 1), (NJ, NJ))
REM = 2 * HALF


def build_dlrm(nc, a):
    fp32 = mybir.dt.float32
    fp32r = mybir.dt.float32r
    i32 = mybir.dt.int32
    ALU = mybir.AluOpType
    ACT = mybir.ActivationFunctionType

    ctx = ExitStack()
    with ctx:
        def sb(name, shape, dt=fp32):
            return ctx.enter_context(nc.sbuf_tensor(name, shape, dt))

        def ps(name, shape):
            return ctx.enter_context(nc.psum_tensor(name, shape, fp32))

        def sem(name):
            return ctx.enter_context(nc.semaphore(name))

        emb = nc.dram_tensor("emb_rows", [WRAP, ROW], fp32, kind="Internal")

        ids_n = sb("ids_n", [PAIRS, GS, PAIR_GATHERS, F], i32)
        ids_f = sb("ids_f", [PAIRS, PAIR_GATHERS, F * GS])
        table_row = sb("table_row", [P, 1])
        idx_all = sb("idx_all", [P, PAIR_GATHERS, PAIRS], i32)
        idx = sb("idx", [P, PAIR_GATHERS], i32)
        gathered = sb("gathered", [P, PAIR_GATHERS, D])
        w1T = sb("w1T", [P, K1, O])
        w1remT = sb("w1remT", [3 * REM, 2, O], fp32r)
        w2T = sb("w2T", [P, len(PLAIN) * NJ, O])
        w2full = sb("w2full", [P, O])
        w2hi = sb("w2hi", [P, len(SPLIT) * NJ, O], fp32r)
        w2lo = sb("w2lo", [P, len(SPLIT) * NJ, O], fp32r)
        w16hi = sb("w16hi", [P, HALF], fp32r)
        bias1 = sb("bias1", [P, 1])
        bias2 = sb("bias2", [P, 1])
        ident = sb("ident", [P, P])
        h0 = [sb(f"h0_{s}", [P, N]) for s in range(2)]
        h0shift = [sb(f"h0shift_{s}", [P, K1, N]) for s in range(2)]
        rem_a = sb("rem_a", [REM, N])
        rem_b = sb("rem_b", [REM, N])
        rem_prod = sb("rem_prod", [REM, N])
        rem_parts = sb("rem_parts", [3 * REM, N], fp32r)
        prod1 = [sb(f"prod1_{s}", [P, K1, N]) for s in range(2)]
        x1 = [sb(f"x1_{s}", [P, N]) for s in range(2)]
        x1rep = [sb(f"x1rep_{s}", [P, NI, N]) for s in range(2)]
        h0rep = [sb(f"h0rep_{s}", [P, NJ, N]) for s in range(2)]
        prod2 = [sb(f"prod2_{n}", [P, 2, NJ, N]) for n in range(2)]
        prod2hi = [sb(f"prod2hi_{n}", [P, NJ, N], fp32r) for n in range(len(SPLIT))]
        prod2lo = [sb(f"prod2lo_{n}", [P, NJ, N], fp32r) for n in range(len(SPLIT))]
        z1 = sb("z1", [P, B])
        z2 = sb("z2", [P, B])
        dense_n = sb("dense_n", [P, BT, DENSE])
        denseT = sb("denseT", [DENSE, B])
        wt1a = sb("wt1a", [P, HID1])
        wt1b = sb("wt1b", [P, HID1])
        wt2 = sb("wt2", [P, HID1 // P, HID2])
        wt3 = sb("wt3", [P, HID2 // P])
        bt1 = sb("bt1", [P, HID1 // P])
        bt2 = sb("bt2", [P, HID2 // P])
        hid1 = [prod2[h][:, 0, :, :] for h in range(2)]
        hid2 = [prod1[h] for h in range(2)]
        y = sb("y", [1, B])

        acc1 = [ps(f"acc1_{s}", [P, N]) for s in range(2)]
        acc2 = [ps(f"acc2_{s}", [P, N]) for s in range(2)]
        tp = [ps(f"tp_{s}", [P, N]) for s in range(2)]
        top_acc = [acc1[0], acc1[1], tp[0], tp[1]]

        w1_in = sem("w1_in")
        weights_in = sem("weights_in")
        ids_in = sem("ids_in")
        ids_float = sem("ids_float")
        ids_turned = sem("ids_turned")
        idx_all_ready = sem("idx_all_ready")
        idx_ready = sem("idx_ready")
        lookups_begun = sem("lookups_begun")
        rows_gathered = sem("rows_gathered")
        emb_stored = sem("emb_stored")
        wt1a_zero = sem("wt1a_zero")
        ident_zero = sem("ident_zero")
        ident_ready = sem("ident_ready")
        w1_folded = sem("w1_folded")
        w2_grouped = sem("w2_grouped")
        weight_step = sem("weight_step")
        tp_filled = sem("tp_filled")
        tp_copied = sem("tp_copied")
        h0_in = [sem(f"h0_in_{s}") for s in range(2)]
        h0rep_in = [sem(f"h0rep_in_{s}") for s in range(2)]
        x1rep_in = [sem(f"x1rep_in_{s}") for s in range(2)]
        rem_in = sem("rem_in")
        rem_prod_ready = sem("rem_prod_ready")
        rem_hi_ready = sem("rem_hi_ready")
        prod1_ready = sem("prod1_ready")
        prod2_ready = sem("prod2_ready")
        hi_ready = sem("hi_ready")
        lo_ready = sem("lo_ready")
        split_used = sem("split_used")
        acc1_ready = sem("acc1_ready")
        x1_ready = sem("x1_ready")
        z2_ready = sem("z2_ready")
        dense_placed = sem("dense_placed")
        top_mm = sem("top_mm")
        top_ready = sem("top_ready")
        y_mm = sem("y_mm")
        y_ready = sem("y_ready")
        y_stored = sem("y_stored")

        WEIGHT_DMAS = 11
        STORES = 16 * 2

        w1n = x1rep[0][:, 0:2, :].rearrange("o a n -> o (a n)")
        w2n = x1rep[1][:, :, :].rearrange("o a n -> o (a n)")
        w1fold = x1rep[0][:, 2, :]
        w16 = x1rep[0][:, 3, 0:HALF]
        w1rem = [x1rep[0][:, 3, P * (s + 1):P * (s + 1) + 3 * REM] for s in range(2)]
        w2r = prod2[0][:, 0, :, :].rearrange("o i (j hm) -> o i j hm", j=NJ)

        def four(t):
            return t.rearrange("p k o -> p (k o)")

        turns1 = [([w1fold[:, k * P:(k + 1) * P] for k in range(K1)], P, [(0, K1 * P, four(w1T[:, :, :]), None)]),
                  (w1rem, 3 * REM, [(0, 2 * P, four(w1remT[:, :, :]), None)])]
        turns2 = [([w2r[:, i, j, :] for j in range(NJ)], P,
                   [(0, NJ * P, four(w2T[:, NJ * n:NJ * (n + 1), :]), None)]) for n, i in enumerate(PLAIN)]
        for n, i in enumerate(SPLIT):
            k = NJ * n
            parts = [(0, NJ * P, four(w2hi[:, k:k + NJ, :]), four(w2lo[:, k:k + NJ, :]))]
            if n == len(SPLIT) - 1:
                parts.append(((NJ - 1) * P, NJ * P, w2full[:, :], None))
            turns2.append(([w2r[:, i, j, :] for j in range(NJ)], P, parts))
        turns2 += [([dense_n[:, 4 * h + t, :] for t in range(4)], DENSE,
                    [(0, N, denseT[:, h * N:(h + 1) * N], None)]) for h in range(2)]

        def software_pipeline(eng, step):
            step(0, 0, 0, True, False)
            step(1, 0, 1, True, False)
            with eng.Fori(1, PAIRS - 1) as pair:
                step(2 * pair, pair, 0, False, False)
                step(2 * pair + 1, pair, 1, False, False)
            step(CHUNKS - 2, PAIRS - 1, 0, False, True)
            step(CHUNKS - 1, PAIRS - 1, 1, False, True)

        block = ctx.enter_context(nc.Block())

        @block.gpsimd
        def _(pool):
            nc.gpsimd.memset(wt1a[0:H, :], 0.0).then_inc(wt1a_zero, 1)
            nc.gpsimd.memset(ident[:, :], 0.0).then_inc(ident_zero, 1)
            pool.wait_ge(ident_zero, 1)
            nc.gpsimd.affine_select(out=ident[:, :], in_=ident[:, :], compare_op=ALU.not_equal, fill=1.0,
                                    base=0, pattern=[[-1, P]], channel_multiplier=1).then_inc(ident_ready, 1)
            pool.wait_ge(idx_all_ready, 1)
            with pool.Fori(0, PAIRS) as pair:
                nc.gpsimd.tensor_copy(idx[:, :].unsqueeze(2), idx_all[:, :, bass.ds(pair, 1)]).then_inc(idx_ready, 1)
                pool.wait_ge(idx_ready, pair + 1)
                pool.sem_inc(lookups_begun, 1)
                for g in range(PAIR_GATHERS):
                    nc.gpsimd.indirect_dma_start(
                        out=gathered[:, g, :], out_offset=None, in_=a["tables"],
                        in_offset=bass.IndirectOffsetOnAxis(ap=idx[:, g:g + 1], axis=0)).then_inc(rows_gathered, 16)
                pool.wait_ge(rows_gathered, 16 * PAIR_GATHERS * pair + 16 * PAIR_GATHERS)
                at = pair * (2 * N)
                for f0, nf in ((0, F), (F, WRAP - F)):
                    dst = bass.AP(emb, f0 * ROW + at, [[ROW, nf], [PAIR_GATHERS * D, GS], [1, PAIR_GATHERS * D]])
                    pool.dma_start(dst, gathered[0:nf * GS, :, :]).then_inc(emb_stored, 16)
                pool.wait_ge(emb_stored, STORES * pair + STORES)

        @block.sync
        def _(sp):
            sp.dma_start(ids_n[:, :, :, :], a["ids"].rearrange("(r q g) f -> r q g f", q=GS, g=PAIR_GATHERS)
                         ).then_inc(ids_in, 16)
            sp.dma_start(table_row[:, :], a["table_rows"]).then_inc(ids_in, 16)
            sp.dma_start(w1n, a["L0_rec_W1"]).then_inc(w1_in, 16)
            sp.dma_start(w2n, a["L0_rec_W2"]).then_inc(weights_in, 16)
            sp.dma_start(bias1[:, :], a["L0_rec_b1"].rearrange("(p one) -> p one", one=1)).then_inc(weights_in, 16)
            sp.dma_start(bias2[:, :], a["L0_rec_b2"].rearrange("(p one) -> p one", one=1)).then_inc(weights_in, 16)
            sp.dma_start(dense_n[:, :, :], a["dense_ctx"].rearrange("(t p) c -> p t c", p=P)).then_inc(weights_in, 16)
            sp.dma_start(wt1a[H:P, :], a["W_top1"][0:O - H, :]).then_inc(weights_in, 16)
            sp.dma_start(wt1b[:, :], a["W_top1"][O - H:2 * O - H, :]).then_inc(weights_in, 16)
            sp.wait_ge(wt1a_zero, 1)
            sp.dma_start(wt1a[0:DENSE, :], a["W_top1"][2 * O - H:2 * O - H + DENSE, :]).then_inc(weights_in, 16)
            sp.dma_start(wt2[:, :, :], a["W_top2"].rearrange("(k p) n -> p k n", p=P)).then_inc(weights_in, 16)
            with nc.allow_non_contiguous_dma(reason="short columns of biases"):
                sp.dma_start(wt3[:, :], a["W_top3"].rearrange("(k p) one -> p (k one)", p=P)).then_inc(weights_in, 16)
                sp.dma_start(bt1[:, :], a["b_top1"].rearrange("(k p) -> p k", p=P)).then_inc(weights_in, 16)
                sp.dma_start(bt2[:, :], a["b_top2"].rearrange("(k p) -> p k", p=P)).then_inc(weights_in, 16)

            def load_h0(col, s):
                sp.dma_start(h0[s][:, :], bass.AP(emb, col, [[ROW, F], [0, SH], [1, N]])).then_inc(h0_in[s], 16)
                for k in range(K1):
                    src = bass.AP(emb, SH * k * ROW + col, [[ROW, F], [ROW, SH], [1, N]])
                    sp.dma_start(h0shift[s][:, k, :], src).then_inc(h0_in[s], 16)

            def load_rem(col):
                for t, f0 in ((rem_a, 0), (rem_b, HALF)):
                    src = bass.AP(emb, f0 * ROW + col, [[ROW, HALF], [N, 2], [1, N]])
                    sp.dma_start(t[:, :], src).then_inc(rem_in, 16)

            def load_h0rep(col, s):
                for j in range(NJ):
                    src = bass.AP(emb, GM * j * ROW + col, [[0, GH], [ROW, GM], [1, N]])
                    sp.dma_start(h0rep[s][:, j, :], src).then_inc(h0rep_in[s], 16)

            def replicate_x1(s):
                for i in range(NI):
                    src = x1[s][GH * i:GH * (i + 1), :].unsqueeze(1).to_broadcast([GH, GM, N])
                    sp.dma_start(x1rep[s][:, i, :], src).then_inc(x1rep_in[s], 16)

            sp.wait_ge(emb_stored, STORES)
            load_rem(0)
            load_h0(0, 0)
            load_h0(N, 1)
            load_h0rep(0, 0)
            sp.wait_ge(x1_ready, 1)
            replicate_x1(0)
            load_h0rep(N, 1)

            def step(c, pair, s, first, last):
                if not last and s == 0:
                    sp.wait_ge(emb_stored, STORES * pair + 2 * STORES)
                if first and s == 0:
                    sp.wait_ge(prod1_ready, 1)
                else:
                    sp.wait_ge(prod2_ready, 2 * c)
                if not last:
                    load_h0((c + 2) * N, s)
                    if s == 0:
                        load_rem((c + 2) * N)
                if not (last and s == 1):
                    sp.wait_ge(x1_ready, c + 2)
                    replicate_x1(1 - s)
                if not last:
                    sp.wait_ge(prod2_ready, 2 * c + 2)
                    load_h0rep((c + 2) * N, s)

            software_pipeline(sp, step)

            sp.wait_ge(y_ready, 2)
            sp.dma_start(a["out"].rearrange("b one -> one b"), y[:, :]).then_inc(y_stored, 16)
            sp.wait_ge(y_stored, 16)

        @block.vector
        def _(dve):
            dve.wait_ge(ids_in, 32)
            nc.vector.tensor_copy(ids_f[:, :, :].rearrange("r g (f q) -> r g f q", q=GS),
                                  ids_n[:, :, :, :].rearrange("r q g f -> r g f q")).then_inc(ids_float, 1)
            dve.wait_ge(ids_turned, 1)
            nc.vector.tensor_scalar(idx_all[:, :, :], tp[0][:, 0:PAIR_GATHERS * PAIRS].rearrange(
                "p (g r) -> p g r", g=PAIR_GATHERS), table_row[:, :], None, ALU.add).then_inc(idx_all_ready, 1)
            dve.wait_ge(w1_in, 16)
            for s in range(K1 * SH):
                for i0, n in ((0, F - s), (F - s, s)):
                    if n == 0:
                        continue
                    m0 = (i0 + s) % F
                    ij, ji = i0 * F + m0, m0 * F + i0
                    c0 = (s // SH) * P + i0 * SH + s % SH
                    dst = w1fold[:, c0:c0 + (n - 1) * SH + 1:SH]
                    x = w1n[:, ij:ij + (n - 1) * (F + 1) + 1:F + 1]
                    if s == 0:
                        nc.vector.tensor_copy(dst, x)
                    else:
                        nc.vector.tensor_tensor(dst, x, w1n[:, ji:ji + (n - 1) * (F + 1) + 1:F + 1], ALU.add)
            ij, ji = HALF, HALF * F
            nc.vector.tensor_tensor(w16, w1n[:, ij:ij + (HALF - 1) * (F + 1) + 1:F + 1],
                                    w1n[:, ji:ji + (HALF - 1) * (F + 1) + 1:F + 1], ALU.add).then_inc(weight_step, 1)
            for s in range(2):
                last = nc.vector.memset(w1rem[s], 0.0)
            last.then_inc(weight_step, 1)
            dve.wait_ge(weight_step, 2)
            nc.vector.tensor_copy(w16hi[:, :], w16).then_inc(weight_step, 1)
            dve.wait_ge(weight_step, 3)
            for u in range(2):
                hi0, lo1, hi2 = (w1rem[u][:, b * REM + u:(b + 1) * REM:2] for b in range(3))
                nc.vector.tensor_copy(hi0, w16hi[:, :].bitcast(fp32))
                nc.vector.tensor_tensor(lo1, w16, w16hi[:, :].bitcast(fp32), ALU.subtract)
                last = nc.vector.tensor_copy(hi2, w16hi[:, :].bitcast(fp32))
            last.then_inc(w1_folded, 1)

            def store_turned(turns, n0):
                parts = 0
                for n, (_, rows, places) in enumerate(turns, n0):
                    dve.wait_ge(tp_filled, n + 1)
                    for c0, c1, dst, lo in places:
                        src = tp[n % 2][0:rows, c0:c1]
                        last = nc.vector.tensor_copy(dst, src)
                        if lo is not None:
                            parts += 1
                            last.then_inc(weight_step, 1)
                            dve.wait_ge(weight_step, 3 + parts)
                            last = nc.vector.tensor_tensor(lo, src, dst.bitcast(fp32), ALU.subtract)
                    last.then_inc(tp_copied, 1)

            store_turned(turns1, 0)

            dve.wait_ge(weights_in, 16 * WEIGHT_DMAS)
            for i in range(NI):
                src = w2n.rearrange("o (i hh j mm) -> o i j hh mm", i=NI, hh=GH, j=NJ)[:, i]
                last = nc.vector.tensor_copy(w2r[:, i].rearrange("o j (hh mm) -> o j hh mm", hh=GH), src)
            last.then_inc(w2_grouped, 1)
            store_turned(turns2, len(turns1))

            def remainder_products(pair):
                dve.wait_ge(rem_in, 32 * pair + 32)
                nc.vector.tensor_tensor(rem_prod[:, :], rem_a[:, :], rem_b[:, :], ALU.mult).then_inc(rem_prod_ready, 1)

            def products1(pair, s):
                dve.wait_ge(h0_in[s], 16 * (K1 + 1) * pair + 16 * (K1 + 1))
                return nc.vector.tensor_tensor(prod1[s][:, :, :], h0shift[s][:, :, :],
                                               h0[s][:, :].unsqueeze(1).to_broadcast([P, K1, N]), ALU.mult)

            def remainder_lo(pair):
                dve.wait_ge(rem_hi_ready, pair + 1)
                return nc.vector.tensor_tensor(rem_parts[2 * REM:3 * REM, :], rem_prod[:, :],
                                               rem_parts[0:REM, :].bitcast(fp32), ALU.subtract)

            remainder_products(0)
            remainder_lo(0)
            products1(0, 0).then_inc(prod1_ready, 1)

            def step(c, pair, s, first, last):
                if not last and s == 1:
                    dve.wait_ge(acc1_ready, c + 1)
                    remainder_products(pair + 1)
                    products1(pair + 1, 0)
                    remainder_lo(pair + 1).then_inc(prod1_ready, 1)
                elif s == 0:
                    if not first:
                        dve.wait_ge(acc1_ready, c)
                    products1(pair, 1).then_inc(prod1_ready, 1)
                dve.wait_ge(h0rep_in[s], 16 * NJ * pair + 16 * NJ)
                dve.wait_ge(x1rep_in[s], 16 * NI * pair + 16 * NI)

                for n in range(2):
                    if not (first and s == 0):
                        dve.wait_ge(split_used, 2 * c + (n - 1))
                    nc.vector.tensor_tensor(
                        prod2[n][:, :, :, :], h0rep[s][:, :, :].unsqueeze(1).to_broadcast([P, 2, NJ, N]),
                        x1rep[s][:, 2 * n:2 * n + 2, :].unsqueeze(2).to_broadcast([P, 2, NJ, N]),
                        ALU.mult).then_inc(prod2_ready, 1)
                for n in range(2):
                    m = SPLIT_J[s][n]
                    dve.wait_ge(hi_ready, 2 * c + (n + 1))
                    nc.vector.tensor_tensor(prod2lo[n][:, 0:m, :], prod2[n][:, 1, 0:m, :],
                                            prod2hi[n][:, 0:m, :].bitcast(fp32), ALU.subtract).then_inc(lo_ready, 1)

            software_pipeline(dve, step)

            dve.wait_ge(x1_ready, CHUNKS)
            nc.vector.memset(z1[0:H, :], 0.0).then_inc(weight_step, 1)
            dve.wait_ge(weight_step, 3 + len(SPLIT) + 1)
            nc.vector.tensor_copy(z1[0:DENSE, :], denseT[:, :]).then_inc(dense_placed, 1)

        @block.tensor
        def _(pe):
            pe.wait_ge(ident_ready, 1)
            pe.wait_ge(ids_float, 1)
            for g in range(PAIR_GATHERS):
                mm = nc.tensor.transpose(tp[0][:, g * PAIRS:(g + 1) * PAIRS], ids_f[:, g, :],
                                         ident[0:PAIRS, 0:PAIRS])
            mm.then_inc(ids_turned, 1)
            pe.wait_ge(idx_all_ready, 1)

            def turn(turns, n0):
                for n, (sources, rows, _) in enumerate(turns, n0):
                    if n >= 2:
                        pe.wait_ge(tp_copied, n - 1)
                    for k, src in enumerate(sources):
                        mm = nc.tensor.transpose(tp[n % 2][0:rows, k * P:(k + 1) * P], src, ident[:, :])
                    mm.then_inc(tp_filled, 1)

            pe.wait_ge(w1_folded, 1)
            turn(turns1, 0)
            pe.wait_ge(w2_grouped, 1)
            turn(turns2, len(turns1))
            pe.wait_ge(tp_copied, len(turns1) + len(turns2))

            def layer1(s):
                for k in range(K1):
                    nc.tensor.matmul(acc1[s][:, :], w1T[:, k, :], prod1[s][:, k, :], start=(k == 0), stop=False)
                nc.tensor.matmul(acc1[s][:, :], w1remT[:, s, :], rem_parts[:, :],
                                 start=False, stop=True).then_inc(acc1_ready, 1)

            pe.wait_ge(prod1_ready, 1)
            layer1(0)

            def step(c, pair, s, first, last):
                if not (last and s == 1):
                    pe.wait_ge(prod1_ready, c + 2)
                    if not (first and s == 0):
                        pe.wait_ge(x1_ready, c)
                    layer1(1 - s)
                if not first:
                    pe.wait_ge(z2_ready, c - 1)
                for n in range(2):
                    pe.wait_ge(prod2_ready, 2 * c + (n + 1))
                    for j in range(NJ):
                        nc.tensor.matmul(acc2[s][:, :], w2T[:, NJ * n + j, :], prod2[n][:, 0, j, :],
                                         start=(n == 0 and j == 0), stop=False)
                for n in range(2):
                    m = SPLIT_J[s][n]
                    pe.wait_ge(hi_ready, 2 * c + (n + 1))
                    for j in range(m):
                        k = NJ * n + j
                        nc.tensor.matmul(acc2[s][:, :], w2lo[:, k, :], prod2hi[n][:, j, :], start=False, stop=False)
                        nc.tensor.matmul(acc2[s][:, :], w2hi[:, k, :], prod2hi[n][:, j, :], start=False, stop=False)
                    if m < NJ:
                        nc.tensor.matmul(acc2[s][:, :], w2full[:, :], prod2[n][:, 1, m, :], start=False, stop=False)
                    pe.wait_ge(lo_ready, 2 * c + (n + 1))
                    for j in range(m):
                        k = NJ * n + j
                        mm = nc.tensor.matmul(acc2[s][:, :], w2hi[:, k, :], prod2lo[n][:, j, :],
                                              start=False, stop=(n == 1 and j == m - 1))
                    mm.then_inc(split_used, 1)

            software_pipeline(pe, step)

            pe.wait_ge(dense_placed, 1)
            for h in range(2):
                cols = slice(h * N, (h + 1) * N)
                pe.wait_ge(z2_ready, (h + 1) * CHUNKS // 2)
                for m in range(M1):
                    n, mc = h * M1 + m, slice(m * P, (m + 1) * P)
                    if n >= len(top_acc):
                        pe.wait_ge(top_ready, n - len(top_acc) + 1)
                    acc = top_acc[n % len(top_acc)]
                    nc.tensor.matmul(acc[:, :], wt1a[:, mc], z1[:, cols], start=True, stop=False)
                    nc.tensor.matmul(acc[:, :], wt1b[:, mc], z2[:, cols], start=False, stop=True).then_inc(top_mm, 1)
            for h in range(2):
                for m in range(M2):
                    n = 2 * M1 + h * M2 + m
                    pe.wait_ge(top_ready, max((h + 1) * M1, n - len(top_acc) + 1))
                    for k in range(M1):
                        mm = nc.tensor.matmul(top_acc[n % len(top_acc)][:, :], wt2[:, k, m * P:(m + 1) * P],
                                              hid1[h][:, k, :], start=(k == 0), stop=(k == M1 - 1))
                    mm.then_inc(top_mm, 1)
            for h in range(2):
                pe.wait_ge(top_ready, 2 * M1 + (h + 1) * M2)
                for k in range(M2):
                    mm = nc.tensor.matmul(acc2[h][0:1, :], wt3[:, k:k + 1], hid2[h][:, k, :],
                                          start=(k == 0), stop=(k == M2 - 1))
                mm.then_inc(y_mm, 1)

        @block.scalar
        def _(act):
            def reduce_relu(acc, bias, out, z, c, ready):
                for b in range(CB):
                    cols = slice(b * D, (b + 1) * D)
                    ins = nc.scalar.activation(out[:, cols], acc[:, cols], ACT.Relu, bias=bias[:, :],
                                               accum_out=z[:, bass.ds(c * CB + b, 1)])
                ins.then_inc(ready, 1)

            def remainder_hi(pair):
                act.wait_ge(rem_prod_ready, pair + 1)
                nc.scalar.copy(rem_parts[0:REM, :], rem_prod[:, :])
                nc.scalar.copy(rem_parts[REM:2 * REM, :], rem_prod[:, :]).then_inc(rem_hi_ready, 1)

            act.wait_ge(ident_ready, 1)
            nc.scalar.activation(y[0:1, 0:1], ident[0:1, 0:1], ACT.Relu)
            act.wait_ge(weights_in, 16 * WEIGHT_DMAS)
            remainder_hi(0)
            act.wait_ge(acc1_ready, 1)
            reduce_relu(acc1[0], bias1, x1[0], z1, 0, x1_ready)

            def step(c, pair, s, first, last):
                def product_hi(n):
                    act.wait_ge(prod2_ready, 2 * c + (n + 1))
                    m = SPLIT_J[s][n]
                    nc.scalar.copy(prod2hi[n][:, 0:m, :], prod2[n][:, 1, 0:m, :]).then_inc(hi_ready, 1)

                if not last and s == 1:
                    remainder_hi(pair + 1)
                if not (first and s == 0):
                    act.wait_ge(split_used, 2 * c)
                    reduce_relu(acc2[1 - s], bias2, acc2[1 - s], z2, c - 1, z2_ready)
                product_hi(0)
                if not (last and s == 1):
                    act.wait_ge(acc1_ready, c + 2)
                    if not (first and s == 0):
                        act.wait_ge(x1rep_in[1 - s], 16 * NI * (pair + s))
                    reduce_relu(acc1[1 - s], bias1, x1[1 - s], z1, c + 1, x1_ready)
                product_hi(1)

            software_pipeline(act, step)
            act.wait_ge(split_used, 2 * CHUNKS)
            reduce_relu(acc2[1], bias2, acc2[1], z2, CHUNKS - 1, z2_ready)

            for layer, (ms, bias, hid) in enumerate(((M1, bt1, hid1), (M2, bt2, hid2))):
                for h in range(2):
                    for m in range(ms):
                        n = layer * 2 * M1 + h * ms + m
                        act.wait_ge(top_mm, n + 1)
                        nc.scalar.activation(hid[h][:, m, :], top_acc[n % len(top_acc)][:, :], ACT.Relu,
                                             bias=bias[:, m:m + 1]).then_inc(top_ready, 1)
            for h in range(2):
                act.wait_ge(y_mm, h + 1)
                nc.scalar.copy(y[0:1, h * N:(h + 1) * N], acc2[h][0:1, :]).then_inc(y_ready, 1)


def kernel(**inputs):
    import numpy as _np
    import concourse.bacc as _bacc
    from concourse import mybir as _mybir
    from concourse.bass_utils import run_bass_kernel_spmd as _run

    nc = _bacc.Bacc("TRN2", target_bir_lowering=False, num_devices=1)
    tables = [_np.asarray(inputs.pop(f"tbl_{f}")) for f in range(F)]
    first_row = _np.cumsum([0] + [t.shape[0] for t in tables[:-1]])
    inputs["tables"] = _np.concatenate(tables, axis=0)
    inputs["table_rows"] = _np.repeat(first_row.astype(_np.float32), GS)[:, None]
    arrays, aps = {}, {}
    for name, value in inputs.items():
        v = _np.ascontiguousarray(value)
        arrays[f"in_{name}"] = v
        aps[name] = nc.dram_tensor(f"in_{name}", v.shape, _mybir.dt.from_np(v.dtype), kind="ExternalInput").ap()
    aps["out"] = nc.dram_tensor("out_y", (B, 1), _mybir.dt.float32, kind="ExternalOutput").ap()
    build_dlrm(nc, aps)
    r = _run(nc, [arrays], core_ids=[0])
    return r.results[0]["out_y"]
```
